# Optimizing a Trainium2 kernel written in Bass

```python
import numpy as np
import jax
import jax.numpy as jnp

def _softmax(x, axis=-1):
    return jax.nn.softmax(x, axis=axis)

def _gelu(x):
    return jax.nn.gelu(x, approximate=True)

def _silu(x):
    return jax.nn.silu(x)

def _sigmoid(x):
    return jax.nn.sigmoid(x)

def _layernorm(x, axis=-1, eps=1e-05):
    m = jnp.mean(x, axis=axis, keepdims=True)
    v = jnp.var(x, axis=axis, keepdims=True)
    return (x - m) / jnp.sqrt(v + eps)

def _scatter_add(tgt, idx, src, axis=0):
    return tgt.at[idx].add(src)

def _segment_sum(src, seg, n):
    return jax.ops.segment_sum(src, seg, n)
kernel_name = 'mk_gnn_resnorm_d1_gnn_r8_a3c55a'

def setup_inputs(seed: int=0):
    np.random.seed(seed)
    _w = jnp.asarray

    def _rec_inputs():
        import jax
        import jax.numpy as jnp
        _gk = jax.random.key(seed)
        x = -0.0003713 + 1 * jax.random.normal(jax.random.fold_in(_gk, 1), (12500, 128), jnp.float32)
        src = jax.random.randint(jax.random.fold_in(_gk, 2), (400000,), 0, 12500, jnp.int32)
        dst = jnp.minimum((12500 * jax.random.uniform(jax.random.fold_in(_gk, 3), (400000,)) ** 2.0).astype(jnp.int32), 99999)
        _o = jnp.argsort(dst, stable=True)
        src = src[_o]
        dst = dst[_o]
        edge_attr_4 = 0.000398945 + 1.00003 * jax.random.normal(jax.random.fold_in(_gk, 11), (400000, 4), jnp.float32)
        return (x, src, dst, edge_attr_4)
    x, src, dst, edge_attr_4 = _rec_inputs()

    def _L0_gnn_setup():
        import jax, jax.numpy as jnp
        import numpy as np
        N = 12500
        E = 200000
        IN_DIM = 128
        OUT_DIM = 128
        EDGE_DIM = 4
        LN_EPS = 1e-05
        key = jax.random.key(seed)
        ks = jax.random.split(key, 12)
        s_in = 1.0 / np.sqrt(IN_DIM)
        s_ed = 1.0 / np.sqrt(EDGE_DIM)
        s_out = 1.0 / np.sqrt(OUT_DIM)
        s_cat = 1.0 / np.sqrt(IN_DIM + OUT_DIM)
        return {'x': jax.random.normal(ks[0], (N, IN_DIM), jnp.float32), 'edge_index': jax.random.randint(ks[1], (2, E), 0, N, jnp.int32), 'edge_attr': jax.random.normal(ks[2], (E, EDGE_DIM), jnp.float32), 'agg_W': jax.random.uniform(ks[3], (IN_DIM, OUT_DIM), jnp.float32, -s_in, s_in), 'agg_b': jnp.zeros((OUT_DIM,), jnp.float32), 'edge_W1': jax.random.uniform(ks[4], (EDGE_DIM, OUT_DIM), jnp.float32, -s_ed, s_ed), 'edge_b1': jnp.zeros((OUT_DIM,), jnp.float32), 'edge_W2': jax.random.uniform(ks[5], (OUT_DIM, 1), jnp.float32, -s_out, s_out), 'edge_b2': jnp.zeros((1,), jnp.float32), 'upd_W1': jax.random.uniform(ks[6], (IN_DIM + OUT_DIM, OUT_DIM), jnp.float32, -s_cat, s_cat), 'upd_b1': jnp.zeros((OUT_DIM,), jnp.float32), 'upd_W2': jax.random.uniform(ks[7], (OUT_DIM, OUT_DIM), jnp.float32, -s_out, s_out), 'upd_b2': jnp.zeros((OUT_DIM,), jnp.float32), 'ln_g': jnp.ones((OUT_DIM,), jnp.float32), 'ln_b': jnp.zeros((OUT_DIM,), jnp.float32), 'res_W': jax.random.uniform(ks[8], (IN_DIM, OUT_DIM), jnp.float32, -s_in, s_in)}
    _L0_gnn_all = _L0_gnn_setup()
    _L0_gnn_in = {k: v for k, v in _L0_gnn_all.items() if k in ('agg_W', 'agg_b', 'edge_W1', 'edge_b1', 'edge_W2', 'edge_b2', 'upd_W1', 'upd_b1', 'upd_W2', 'upd_b2', 'ln_g', 'ln_b', 'res_W')}
    del _L0_gnn_all
    return {'x': x, 'src': src, 'dst': dst, 'edge_attr_4': edge_attr_4, 'L0_gnn_agg_W': _L0_gnn_in['agg_W'], 'L0_gnn_agg_b': _L0_gnn_in['agg_b'], 'L0_gnn_edge_W1': _L0_gnn_in['edge_W1'], 'L0_gnn_edge_b1': _L0_gnn_in['edge_b1'], 'L0_gnn_edge_W2': _L0_gnn_in['edge_W2'], 'L0_gnn_edge_b2': _L0_gnn_in['edge_b2'], 'L0_gnn_upd_W1': _L0_gnn_in['upd_W1'], 'L0_gnn_upd_b1': _L0_gnn_in['upd_b1'], 'L0_gnn_upd_W2': _L0_gnn_in['upd_W2'], 'L0_gnn_upd_b2': _L0_gnn_in['upd_b2'], 'L0_gnn_ln_g': _L0_gnn_in['ln_g'], 'L0_gnn_ln_b': _L0_gnn_in['ln_b'], 'L0_gnn_res_W': _L0_gnn_in['res_W']}

def reference(x, src, dst, edge_attr_4, L0_gnn_agg_W, L0_gnn_agg_b, L0_gnn_edge_W1, L0_gnn_edge_b1, L0_gnn_edge_W2, L0_gnn_edge_b2, L0_gnn_upd_W1, L0_gnn_upd_b1, L0_gnn_upd_W2, L0_gnn_upd_b2, L0_gnn_ln_g, L0_gnn_ln_b, L0_gnn_res_W):
    import jax
    import jax.numpy as jnp

    def _L0_gnn_ref(x, edge_index, edge_attr, agg_W, agg_b, edge_W1, edge_b1, edge_W2, edge_b2, upd_W1, upd_b1, upd_W2, upd_b2, ln_g, ln_b, res_W):
        import jax, jax.numpy as jnp
        import numpy as np
        N = 12500
        E = 200000
        IN_DIM = 128
        OUT_DIM = 128
        EDGE_DIM = 4
        LN_EPS = 1e-05
        n = x.shape[0]
        src, dst = (edge_index[0], edge_index[1])
        e_h = jax.nn.silu(edge_attr @ edge_W1 + edge_b1)
        e_w = jax.nn.sigmoid(e_h @ edge_W2 + edge_b2)
        x_agg = jax.nn.silu(x[src] @ agg_W + agg_b) * e_w
        out = jax.ops.segment_sum(x_agg, dst, num_segments=n)
        cnt = jax.ops.segment_sum(jnp.ones((dst.shape[0],), x.dtype), dst, num_segments=n)
        out = out / jnp.maximum(cnt, 1.0)[:, None]
        h = jnp.concatenate([x, out], axis=-1)
        h = jax.nn.silu(h @ upd_W1 + upd_b1) @ upd_W2 + upd_b2
        h = h + x @ res_W
        mu = jnp.mean(h, axis=-1, keepdims=True)
        var = jnp.mean(jnp.square(h - mu), axis=-1, keepdims=True)
        h = (h - mu) * jax.lax.rsqrt(var + LN_EPS) * ln_g + ln_b
        return h
    edge_index = jnp.stack([src, dst])
    x = _layernorm(x + _L0_gnn_ref(x, edge_index, edge_attr_4, L0_gnn_agg_W, L0_gnn_agg_b, L0_gnn_edge_W1, L0_gnn_edge_b1, L0_gnn_edge_W2, L0_gnn_edge_b2, L0_gnn_upd_W1, L0_gnn_upd_b1, L0_gnn_upd_W2, L0_gnn_upd_b2, L0_gnn_ln_g, L0_gnn_ln_b, L0_gnn_res_W), axis=-1)
    return x

_drawn_inputs = setup_inputs


def setup_inputs(seed=0):
    import zlib

    import numpy as np

    out = dict(_drawn_inputs(seed))
    spreads = {'L0_gnn_agg_b': (0.0, 0.8),
     'L0_gnn_edge_b1': (0.0, 0.8),
     'L0_gnn_upd_b1': (0.0, 0.1),
     'L0_gnn_upd_b2': (0.0, 0.1),
     'L0_gnn_ln_g': (1.0, 0.2),
     'L0_gnn_ln_b': (0.0, 0.1)}
    factors = {'edge_attr_4': 8.0, 'L0_gnn_agg_W': 8.0, 'L0_gnn_edge_W1': 8.0, 'L0_gnn_edge_W2': 8.0}
    for name, (base, spread) in spreads.items():
        noise = np.random.default_rng([zlib.crc32(name.encode()), seed]).standard_normal(out[name].shape)
        drawn = base * np.exp(spread * noise) if base else spread * noise
        out[name] = jnp.asarray(drawn.astype(out[name].dtype))
    for name, factor in factors.items():
        out[name] = (out[name] * factor).astype(out[name].dtype)
    return out
```

```python
from contextlib import ExitStack

import concourse.bass as bass
from concourse import mybir


def gnn_layer(nc, x, src, dst, edge_attr, agg_w, agg_b, edge_w1, edge_b1, edge_w2, edge_b2,
              upd_w1, upd_b1, upd_w2, upd_b2, ln_g, ln_b, res_w, out):
    F32 = mybir.dt.float32
    I32 = mybir.dt.int32
    ALU = mybir.AluOpType
    ACT = mybir.ActivationFunctionType
    AX = mybir.AxisListType

    P = 128
    N, D = x.shape
    E, A = edge_attr.shape
    J = 25
    C = E // (P * J)
    W = -(-N // P)
    TAIL = N - (W - 1) * P
    GW = 4
    G = W // GW
    GL = W - G * GW
    S = 5
    T = J // S
    HG = -(-J // GW)
    DC = D + 1
    EPS = 1e-5
    assert C * P * J == E and C % 2 == 1 and G % 2 == 0 and GL == 2 and J % S == 0

    z_dram = nc.dram_tensor("z_nodes", [N, D], F32).ap()

    src_c = src.rearrange("(c p j) -> c p j", p=P, j=J)
    dst_c = dst.rearrange("(c p j) -> c p j", p=P, j=J)
    dst_rows = dst.rearrange("(c e) -> c e", e=P * J)
    attr_c = edge_attr.rearrange("(c p j) a -> c p (j a)", p=P, j=J)

    def group_rows(t, i):
        return t[bass.ds(i * (GW * P), GW * P), :].rearrange("(w p) f -> p w f", p=P)

    ctx = ExitStack()
    with ctx:
        def sb(name, shape, dt=F32):
            return ctx.enter_context(nc.sbuf_tensor(name, shape, dt))

        def sem(name):
            return ctx.enter_context(nc.semaphore(name))

        ident = sb("ident", [P, P])
        iota_i = sb("iota_i", [P, P], I32)
        iota_f = sb("iota_f", [P, P])
        base_i = sb("base_i", [P, W], I32)
        base_f = sb("base_f", [P, W])
        w_agg = sb("w_agg", [P, D])
        w_u1x = sb("w_u1x", [P, D])
        w_u1a = sb("w_u1a", [P, D])
        w_u2 = sb("w_u2", [P, D])
        w_res = sb("w_res", [P, D])
        w_e1 = sb("w_e1", [J * A, J, D])
        w_e2 = sb("w_e2", [P, 1])
        b_agg = sb("b_agg", [P, 1])
        b_e1 = sb("b_e1", [P, 1])
        b_e2 = sb("b_e2", [P, 1])
        b_e2h = sb("b_e2h", [P, 1])
        b_u1 = sb("b_u1", [P, 1])
        b_u2 = sb("b_u2", [P, 1])
        g_row = sb("g_row", [P, D])
        b_row = sb("b_row", [P, D])
        minus_half = sb("minus_half", [P, GW])
        xT = sb("xT", [P, W * P])
        x_in = [sb(f"x_in{p}", [P, GW, D]) for p in range(2)]
        yT = [sb(f"yT{p}", [P, GW * P]) for p in range(2)]
        z_sb = [sb(f"z_sb{p}", [P, GW, D]) for p in range(2)]
        dst_tab = sb("dst_tab", [C, P * J], I32)
        mm_f = sb("mm_f", [C, 2])
        mm_i = sb("mm_i", [C, 2], I32)
        mm_w = sb("mm_w", [C, 2], I32)
        span_f = sb("span_f", [C, 2])
        span_i = sb("span_i", [1, C, 2], I32)
        src_sb = [sb(f"src_sb{p}", [P, J], I32) for p in range(2)]
        dst_sb = [sb(f"dst_sb{p}", [P, J], I32) for p in range(2)]
        attr_sb = [sb(f"attr_sb{p}", [P, J * A]) for p in range(2)]
        attrT = sb("attrT", [J * A, P])
        e_h = [sb(f"e_h{p}", [P, GW * P]) for p in range(2)]
        tanh_e = [sb(f"tanh_e{p}", [P, J]) for p in range(2)]
        e_w = sb("e_w", [P, J])
        dst_f = sb("dst_f", [P, J])
        dst_loc = sb("dst_loc", [P, J])
        ring = sb("ring", [P, J, D])
        msg = sb("msg", [P, J, DC])
        onehot = sb("onehot", [P, J, P])
        acc = sb("acc", [P, W, DC])
        cnt = sb("cnt", [P, W])
        rcnt = sb("rcnt", [P, W])
        agg_n = [sb(f"agg_n{p}", [P, GW, D]) for p in range(2)]
        hT = [sb(f"hT{p}", [P, GW * P]) for p in range(2)]
        stats = sb("stats", [P, GW, 6])
        mv = sb("mv", [P, GW, 2])
        var_e = sb("var_e", [P, GW])
        rstd = sb("rstd", [P, GW])
        res = [sb(f"res{p}", [P, GW, D]) for p in range(2)]

        bank = [ctx.enter_context(nc.psum_tensor(f"bank{b}", [P, 512], F32)) for b in range(8)]
        psXT, psA, psZ = bank[0:2], bank[2:4], bank[4:6]
        psAttr, psEw, psHid, psAgg, psTab = bank[0], bank[1], bank[2:4], bank[4], bank[6]
        psU, psH, psN = bank[0:2], bank[2:4], bank[4:6]

        w_in = sem("w_in")
        attrw_in = sem("attrw_in")
        w_e1_zero = sem("w_e1_zero")
        pool_const = sem("pool_const")
        tab_in = sem("tab_in")
        x_ready = [sem(f"x_ready{p}") for p in range(2)]
        tail_zero = sem("tail_zero")
        xT_mm = sem("xT_mm")
        xT_ready = sem("xT_ready")
        a_mm = sem("a_mm")
        yT_ready = sem("yT_ready")
        z_mm = sem("z_mm")
        z_ready = sem("z_ready")
        z_out = [sem(f"z_out{p}") for p in range(2)]
        dve_step = sem("dve_step")
        span_f_ready = sem("span_f_ready")
        span_mm = sem("span_mm")
        span_ready = sem("span_ready")
        src_in = [sem(f"src_in{p}") for p in range(2)]
        dst_in = [sem(f"dst_in{p}") for p in range(2)]
        attr_in = [sem(f"attr_in{p}") for p in range(2)]
        attr_mm = sem("attr_mm")
        attrT_ready = sem("attrT_ready")
        hid_mm = sem("hid_mm")
        e_h_ready = sem("e_h_ready")
        ew_mm = sem("ew_mm")
        tanh_ready = sem("tanh_ready")
        e_w_ready = sem("e_w_ready")
        dst_f_ready = sem("dst_f_ready")
        gathered = [sem(f"gathered{s}") for s in range(S)]
        scaled = sem("scaled")
        loc_ready = sem("loc_ready")
        onehot_ready = sem("onehot_ready")
        onehot_used = sem("onehot_used")
        acc_added = sem("acc_added")
        rcnt_ready = sem("rcnt_ready")
        agg_ready = sem("agg_ready")
        u_mm = sem("u_mm")
        u_ready = sem("u_ready")
        h_mm = sem("h_mm")
        hT_ready = sem("hT_ready")
        n_mm = sem("n_mm")
        ln_step = sem("ln_step")
        var_ready = sem("var_ready")
        rstd_ready = sem("rstd_ready")
        res_ready = sem("res_ready")
        res_out = [sem(f"res_out{p}") for p in range(2)]
        xo_in = [sem(f"xo_in{p}") for p in range(2)]

        WEIGHTS_IN = 16 * (6 + 4 + 1 + 2)
        XR0 = 16 * (G // 2)

        block = ctx.enter_context(nc.Block())

        @block.sync
        def _(sp):
            weights = [(w_agg[:, :], agg_w), (w_u1x[:, :], upd_w1[0:D, :]), (w_u1a[:, :], upd_w1[D:2 * D, :]),
                       (w_u2[:, :], upd_w2), (w_res[:, :], res_w), (w_e2[:, :], edge_w2)]
            columns = [(b_agg, agg_b), (b_e1, edge_b1), (b_u1, upd_b1), (b_u2, upd_b2)]

            def load_x(i, p):
                if not (isinstance(i, int) and i < 2):
                    sp.wait_ge(xT_mm, i - 1)
                sp.dma_start(x_in[p][:, :, :], group_rows(x, i)).then_inc(x_ready[p], 16)

            for to, of in weights:
                sp.dma_start(to, of).then_inc(w_in, 16)
            for to, of in columns:
                sp.dma_start(to[:, :], of.rearrange("(p o) -> p o", o=1)).then_inc(w_in, 16)
            sp.dma_start(b_e2[:, :], edge_b2.rearrange("(o n) -> o n", o=1).to_broadcast([P, 1])).then_inc(w_in, 16)
            for to, of in ((g_row, ln_g), (b_row, ln_b)):
                sp.dma_start(to[:, :], of.rearrange("(o n) -> o n", o=1).to_broadcast([P, D])).then_inc(w_in, 16)
            load_x(0, 0)
            load_x(1, 1)
            R = C // 8 * 8
            sp.dma_start(dst_tab[0:R, :], dst_rows[0:R, :]).then_inc(tab_in, 16)
            sp.dma_start(dst_tab[R:C, :], dst_rows[R:C, :]).then_inc(tab_in, 16)
            with sp.Fori(2, G - 1, 2) as g:
                load_x(g, 0)
                load_x(g + 1, 1)
            sp.wait_ge(tail_zero, 1)
            lo = G * GW * P
            sp.dma_start(x_in[0][:, 0, :], x[lo:lo + P, :]).then_inc(x_ready[0], 16)
            sp.dma_start(x_in[0][0:TAIL, 1, :], x[lo + P:N, :]).then_inc(x_ready[0], 16)

            def load_chunk(c, p):
                first = isinstance(c, int) and c < 2
                if not first:
                    sp.wait_ge(attr_mm, c - 1)
                sp.dma_start(attr_sb[p][:, :], attr_c[bass.ds(c, 1), :, :].rearrange("o p j -> (o p) j")).then_inc(attr_in[p], 16)
                if not first:
                    sp.wait_ge(scaled, S * (c - 1))
                sp.dma_start(src_sb[p][:, :], src_c[bass.ds(c, 1), :, :].rearrange("o p j -> (o p) j")).then_inc(src_in[p], 16)
                if not first:
                    sp.wait_ge(dst_f_ready, c - 1)
                sp.dma_start(dst_sb[p][:, :], dst_c[bass.ds(c, 1), :, :].rearrange("o p j -> (o p) j")).then_inc(dst_in[p], 16)

            load_chunk(0, 0)
            load_chunk(1, 1)
            with sp.Fori(2, C - 2, 2) as c:
                load_chunk(c, 0)
                load_chunk(c + 1, 1)
            load_chunk(C - 1, 0)

            def load_xo(i, p, last=False):
                if isinstance(i, int) and i < 2:
                    if i == 0:
                        sp.wait_ge(xT_mm, G + 1)
                else:
                    sp.wait_ge(res_ready, i - 1)
                if last:
                    sp.dma_start(x_in[p][:, 0, :], x[lo:lo + P, :]).then_inc(xo_in[p], 16)
                    sp.dma_start(x_in[p][0:TAIL, 1, :], x[lo + P:N, :]).then_inc(xo_in[p], 16)
                else:
                    sp.dma_start(x_in[p][:, :, :], group_rows(x, i)).then_inc(xo_in[p], 16)

            load_xo(0, 0)
            load_xo(1, 1)
            with sp.Fori(2, G - 1, 2) as g:
                load_xo(g, 0)
                load_xo(g + 1, 1)
            load_xo(G, 0, last=True)

        @block.gpsimd
        def _(pool):
            nc.gpsimd.iota(iota_i[:, :], [[1, P]], base=0, channel_multiplier=0).then_inc(pool_const, 1)
            nc.gpsimd.iota(base_i[:, :], [[P, W]], base=0, channel_multiplier=0).then_inc(pool_const, 1)
            nc.gpsimd.memset(ident[:, :], 0.0).then_inc(pool_const, 1)
            pool.wait_ge(pool_const, 3)
            nc.gpsimd.affine_select(out=ident[:, :], in_=ident[:, :], compare_op=ALU.not_equal, fill=1.0, base=0,
                                    pattern=[[-1, P]], channel_multiplier=1).then_inc(pool_const, 1)
            nc.gpsimd.memset(minus_half[:, :], -0.5).then_inc(pool_const, 1)
            pool.wait_ge(z_out[0], XR0 + 32)
            pool.wait_ge(z_out[1], XR0)

            read = pool.alloc_register("segments_read")
            pool.reg_mov(read, 0)

            def gather_chunk(c, p):
                pool.wait_ge(src_in[p], 8 * (c - p) + 16)
                for s in range(S):
                    if not (isinstance(c, int) and c < 1):
                        pool.reg_add(read, read, 1)
                        pool.wait_ge(pool_const, 5)
                        pool.wait_ge(scaled, read)
                    for j in range(s * T, s * T + T):
                        nc.gpsimd.indirect_dma_start(
                            out=ring[:, j, :], out_offset=None, in_=z_dram[:, :],
                            in_offset=bass.IndirectOffsetOnAxis(ap=src_sb[p][:, j:j + 1], axis=0),
                        ).then_inc(gathered[s], 16)

            gather_chunk(0, 0)
            gather_chunk(1, 1)
            with pool.Fori(2, C - 2, 2) as c:
                gather_chunk(c, 0)
                gather_chunk(c + 1, 1)
            gather_chunk(C - 1, 0)

            def inv_std(k, nw):
                pool.wait_ge(var_ready, k)
                nc.gpsimd.tensor_tensor(rstd[:, 0:nw], var_e[:, 0:nw], minus_half[:, 0:nw],
                                        ALU.pow).then_inc(rstd_ready, 1)

            inv_std(1, GW)
            inv_std(2, GW)
            with pool.Fori(1, G, 1) as i:
                inv_std(2 * i + 1, GW)
                inv_std(2 * i + 2, GW)
            inv_std(2 * G + 1, GL)
            inv_std(2 * G + 2, GL)

        @block.scalar
        def _(act):
            act.wait_ge(w_e1_zero, 1)
            for j in range(J):
                act.dma_start(w_e1[A * j:A * j + A, j, :], edge_w1).then_inc(attrw_in, 16)
            act.wait_ge(w_in, WEIGHTS_IN)

            def node_step(i, p, last=False):
                n = GL * P if last else GW * P
                act.wait_ge(a_mm, i + 1)
                if not (isinstance(i, int) and i < 2):
                    act.wait_ge(z_mm, i - 1)
                nc.scalar.activation(yT[p][:, 0:n], psA[p][:, 0:n], ACT.Silu, bias=b_agg[:, :]).then_inc(yT_ready, 1)

            def store_z(i, p, last=False):
                act.wait_ge(z_ready, i + 1)
                if last:
                    lo = G * GW * P
                    act.dma_start(z_dram[lo:lo + P, :], z_sb[p][:, 0, :]).then_inc(z_out[p], 16)
                    act.dma_start(z_dram[lo + P:N, :], z_sb[p][0:TAIL, 1, :]).then_inc(z_out[p], 16)
                else:
                    act.dma_start(group_rows(z_dram, i), z_sb[p][:, :, :]).then_inc(z_out[p], 16)

            node_step(0, 0)
            node_step(1, 1)
            with act.Fori(2, G - 1, 2) as g:
                node_step(g, 0)
                store_z(g - 2, 0)
                node_step(g + 1, 1)
                store_z(g - 1, 1)
            node_step(G, 0, last=True)
            store_z(G - 2, 0)
            store_z(G - 1, 1)
            store_z(G, 0, last=True)

            act.wait_ge(e_w_ready, 1)

            def edge_step(c, p):
                later = not (isinstance(c, int) and c < 1)
                act.wait_ge(attr_mm, c + 1)
                if later:
                    act.wait_ge(hid_mm, HG * c)
                nc.scalar.copy(attrT[:, :], psAttr[0:J * A, 0:P]).then_inc(attrT_ready, 1)
                for g in range(HG):
                    n = min(GW, J - g * GW) * P
                    act.wait_ge(hid_mm, HG * c + g + 1)
                    if g >= 2:
                        act.wait_ge(ew_mm, HG * c + g - 1)
                    elif later:
                        act.wait_ge(ew_mm, HG * c)
                    nc.scalar.activation(e_h[g % 2][:, 0:n], psHid[g % 2][:, 0:n], ACT.Silu,
                                         bias=b_e1[:, :]).then_inc(e_h_ready, 1)
                act.wait_ge(ew_mm, HG * c + HG)
                if not (isinstance(c, int) and c < 2):
                    act.wait_ge(e_w_ready, c)
                nc.scalar.activation(tanh_e[p][:, :], psEw[:, 0:J], ACT.Tanh, bias=b_e2h[:, :],
                                     scale=0.5).then_inc(tanh_ready, 1)

            edge_step(0, 0)
            edge_step(1, 1)
            with act.Fori(2, C - 2, 2) as c:
                edge_step(c, 0)
                edge_step(c + 1, 1)
            edge_step(C - 1, 0)

            def out_step(i, p, last=False):
                n = GL * P if last else GW * P
                act.wait_ge(u_mm, i + 1)
                if not (isinstance(i, int) and i < 2):
                    act.wait_ge(h_mm, i - 1)
                nc.scalar.activation(yT[p][:, 0:n], psU[p][:, 0:n], ACT.Silu, bias=b_u1[:, :]).then_inc(u_ready, 1)
                act.wait_ge(h_mm, i + 1)
                if not (isinstance(i, int) and i < 2):
                    act.wait_ge(n_mm, i - 1)
                nc.scalar.activation(hT[p][:, 0:n], psH[p][:, 0:n], ACT.Identity, bias=b_u2[:, :]).then_inc(hT_ready, 1)

            def store_res(i, p, last=False):
                act.wait_ge(res_ready, i + 1)
                if last:
                    lo = G * GW * P
                    act.dma_start(out[lo:lo + P, :], res[p][:, 0, :]).then_inc(res_out[p], 16)
                    act.dma_start(out[lo + P:N, :], res[p][0:TAIL, 1, :]).then_inc(res_out[p], 16)
                else:
                    act.dma_start(group_rows(out, i), res[p][:, :, :]).then_inc(res_out[p], 16)

            out_step(0, 0)
            out_step(1, 1)
            with act.Fori(2, G - 1, 2) as g:
                out_step(g, 0)
                store_res(g - 2, 0)
                out_step(g + 1, 1)
                store_res(g - 1, 1)
            out_step(G, 0, last=True)
            store_res(G - 2, 0)
            store_res(G - 1, 1)
            store_res(G, 0, last=True)
            act.wait_ge(res_out[0], XR0 + 32)
            act.wait_ge(res_out[1], XR0)

        @block.tensor
        def _(pe):
            pe.wait_ge(pool_const, 5)
            pe.wait_ge(w_in, WEIGHTS_IN)
            pe.wait_ge(attrw_in, 16 * J)

            def transpose_x(i, p, last=False):
                pe.wait_ge(x_ready[p], (XR0 + 32) if last else 8 * (i - p) + 16)
                if not (isinstance(i, int) and i < 2):
                    pe.wait_ge(xT_ready, i - 1)
                for w in range(GL if last else GW):
                    mm = nc.tensor.transpose(psXT[p][:, w * P:w * P + P], x_in[p][:, w, :], ident[:, :])
                mm.then_inc(xT_mm, 1)

            def project_x(i, p, last=False):
                n = GL * P if last else GW * P
                pe.wait_ge(xT_ready, i + 1)
                if not (isinstance(i, int) and i < 2):
                    pe.wait_ge(yT_ready, i - 1)
                nc.tensor.matmul(psA[p][:, 0:n], w_agg[:, :], xT[:, bass.ds(i * (GW * P), n)],
                                 start=True, stop=True).then_inc(a_mm, 1)

            def make_z(i, p, last=False):
                pe.wait_ge(yT_ready, i + 1)
                if not (isinstance(i, int) and i < 2):
                    pe.wait_ge(z_ready, i - 1)
                for w in range(GL if last else GW):
                    mm = nc.tensor.matmul(psZ[p][:, w * P:w * P + P], yT[p][:, w * P:w * P + P], w_u1a[:, :],
                                          start=True, stop=True)
                mm.then_inc(z_mm, 1)

            transpose_x(0, 0)
            transpose_x(1, 1)
            project_x(0, 0)
            transpose_x(2, 0)
            project_x(1, 1)
            make_z(0, 0)
            transpose_x(3, 1)
            project_x(2, 0)
            make_z(1, 1)
            with pe.Fori(4, G - 1, 2) as g:
                transpose_x(g, 0)
                project_x(g - 1, 1)
                make_z(g - 2, 0)
                transpose_x(g + 1, 1)
                project_x(g, 0)
                make_z(g - 1, 1)
            transpose_x(G, 0, last=True)
            project_x(G - 1, 1)
            make_z(G - 2, 0)
            project_x(G, 0, last=True)
            make_z(G - 1, 1)
            make_z(G, 0, last=True)

            pe.wait_ge(span_f_ready, 2)
            for k in range(2):
                mm = nc.tensor.matmul(psTab[0:1, k * P:k * P + C], span_f[:, k:k + 1], ident[0:C, 0:C],
                                      start=True, stop=True)
            mm.then_inc(span_mm, 1)

            def edge_net(c, p):
                later = not (isinstance(c, int) and c < 1)
                pe.wait_ge(attr_in[p], 8 * (c - p) + 16)
                if later:
                    pe.wait_ge(attrT_ready, c)
                nc.tensor.transpose(psAttr[0:J * A, 0:P], attr_sb[p][:, :], ident[:, :]).then_inc(attr_mm, 1)
                pe.wait_ge(attrT_ready, c + 1)
                if later:
                    pe.wait_ge(e_h_ready, HG * c)

                def hidden(g):
                    js = range(g * GW, min(J, g * GW + GW))
                    for j in js:
                        mm = nc.tensor.matmul(psHid[g % 2][:, (j % GW) * P:(j % GW) * P + P], w_e1[:, j, :],
                                              attrT[:, :], start=True, stop=True)
                    mm.then_inc(hid_mm, 1)

                hidden(0)
                hidden(1)
                if later:
                    pe.wait_ge(tanh_ready, c)
                for g in range(HG):
                    pe.wait_ge(e_h_ready, HG * c + g + 1)
                    for j in range(g * GW, min(J, g * GW + GW)):
                        mm = nc.tensor.matmul(psEw[:, j:j + 1], e_h[g % 2][:, (j % GW) * P:(j % GW) * P + P],
                                              w_e2[:, :], start=True, stop=True)
                    mm.then_inc(ew_mm, 1)
                    if g + 2 < HG:
                        hidden(g + 2)

            visit = pe.alloc_register("pe_visit")
            pe.reg_mov(visit, 0)
            win = [pe.alloc_register("pe_win_lo"), pe.alloc_register("pe_win_hi")]

            def aggregate(c):
                pe.wait_ge(scaled, S * c + S)
                pe.load(win, span_i[0:1, bass.ds(c, 1), :])
                lo = pe.snap(win[0], min_val=0, max_val=W - 1)
                hi = pe.snap(win[1], min_val=1, max_val=W)
                with pe.Fori(lo, hi, 1) as w:
                    v = pe.snap(visit, min_val=0, max_val=W * C)
                    pe.wait_ge(acc_added, v + 1)
                    for s in range(S):
                        pe.wait_ge(onehot_ready, v * S + s + 1)
                        for j in range(s * T, s * T + T):
                            mm = nc.tensor.matmul(psAgg[:, 0:DC], onehot[:, j, :], msg[:, j, :],
                                                  start=(j == 0), stop=(j == J - 1))
                        mm.then_inc(onehot_used, 1)
                    pe.reg_add(visit, visit, 1)

            edge_net(0, 0)
            pe.wait_ge(span_ready, 2)
            edge_net(1, 1)
            aggregate(0)
            with pe.Fori(1, C - 3, 2) as c:
                edge_net(c + 1, 0)
                aggregate(c)
                edge_net(c + 2, 1)
                aggregate(c + 1)
            edge_net(C - 1, 0)
            aggregate(C - 2)
            aggregate(C - 1)

            def update1(i, p, last=False):
                nw = GL if last else GW
                pe.wait_ge(agg_ready, i + 1)
                if not (isinstance(i, int) and i < 2):
                    pe.wait_ge(u_ready, i - 1)
                nc.tensor.matmul(psU[p][:, 0:nw * P], w_u1x[:, :], xT[:, bass.ds(i * (GW * P), nw * P)],
                                 start=True, stop=False)
                for w in range(nw):
                    mm = nc.tensor.matmul(psU[p][:, w * P:w * P + P], agg_n[p][:, w, :], ident[:, :],
                                          start=False, stop=(w == nw - 1))
                mm.then_inc(u_mm, 1)

            def update2(i, p, last=False):
                nw = GL if last else GW
                pe.wait_ge(u_ready, i + 1)
                if not (isinstance(i, int) and i < 2):
                    pe.wait_ge(hT_ready, i - 1)
                nc.tensor.matmul(psH[p][:, 0:nw * P], w_res[:, :], xT[:, bass.ds(i * (GW * P), nw * P)],
                                 start=True, stop=False)
                nc.tensor.matmul(psH[p][:, 0:nw * P], w_u2[:, :], yT[p][:, 0:nw * P],
                                 start=False, stop=True).then_inc(h_mm, 1)

            def transpose_h(i, p, last=False):
                pe.wait_ge(hT_ready, i + 1)
                if not (isinstance(i, int) and i < 2):
                    pe.wait_ge(var_ready, i * 2 - 2)
                for w in range(GL if last else GW):
                    mm = nc.tensor.transpose(psN[p][:, w * P:w * P + P], hT[p][:, w * P:w * P + P], ident[:, :])
                mm.then_inc(n_mm, 1)

            update1(0, 0)
            update1(1, 1)
            update2(0, 0)
            update1(2, 0)
            update2(1, 1)
            transpose_h(0, 0)
            update1(3, 1)
            update2(2, 0)
            transpose_h(1, 1)
            with pe.Fori(4, G - 1, 2) as g:
                update1(g, 0)
                update2(g - 1, 1)
                transpose_h(g - 2, 0)
                update1(g + 1, 1)
                update2(g, 0)
                transpose_h(g - 1, 1)
            update1(G, 0, last=True)
            update2(G - 1, 1)
            transpose_h(G - 2, 0)
            update2(G, 0, last=True)
            transpose_h(G - 1, 1)
            transpose_h(G, 0, last=True)

        @block.vector
        def _(dve):
            nc.vector.memset(w_e1[:, :, :], 0.0).then_inc(w_e1_zero, 1)
            nc.vector.memset(acc[:, :, :], 0.0).then_inc(dve_step, 1)
            nc.vector.memset(msg[:, :, D:DC], 1.0).then_inc(dve_step, 1)
            dve.wait_ge(pool_const, 5)
            nc.vector.tensor_copy(iota_f[:, :], iota_i[:, :]).then_inc(dve_step, 1)
            nc.vector.tensor_copy(base_f[:, :], base_i[:, :]).then_inc(dve_step, 1)
            dve.wait_ge(w_in, WEIGHTS_IN)
            nc.vector.tensor_scalar(b_e2h[:, :], b_e2[:, :], 0.5, None, ALU.mult).then_inc(e_w_ready, 1)

            def evacuate_xT(i, p, last=False):
                n = GL * P if last else GW * P
                dve.wait_ge(xT_mm, i + 1)
                nc.vector.tensor_copy(xT[:, bass.ds(i * (GW * P), n)], psXT[p][:, 0:n]).then_inc(xT_ready, 1)

            def evacuate_z(i, p, last=False):
                nw = GL if last else GW
                dve.wait_ge(z_mm, i + 1)
                if not (isinstance(i, int) and i < 2):
                    dve.wait_ge(z_out[p], 8 * (i - p))
                nc.vector.tensor_copy(z_sb[p][:, 0:nw, :].rearrange("p w f -> p (w f)"),
                                      psZ[p][:, 0:nw * P]).then_inc(z_ready, 1)

            evacuate_xT(0, 0)
            evacuate_xT(1, 1)
            evacuate_xT(2, 0)
            evacuate_z(0, 0)
            evacuate_xT(3, 1)
            evacuate_z(1, 1)
            with dve.Fori(4, G - 1, 2) as g:
                evacuate_xT(g, 0)
                evacuate_z(g - 2, 0)
                evacuate_xT(g + 1, 1)
                evacuate_z(g - 1, 1)
            nc.vector.memset(x_in[0][:, 1, :], 0.0).then_inc(tail_zero, 1)
            evacuate_xT(G, 0, last=True)
            evacuate_z(G - 2, 0)
            evacuate_z(G - 1, 1)
            evacuate_z(G, 0, last=True)

            dve.wait_ge(tab_in, 32)
            nc.vector.tensor_reduce(mm_f[:, 0:1], dst_tab[:, :], AX.X, ALU.min).then_inc(dve_step, 1)
            nc.vector.tensor_reduce(mm_f[:, 1:2], dst_tab[:, :], AX.X, ALU.max).then_inc(dve_step, 1)
            dve.wait_ge(dve_step, 6)
            nc.vector.tensor_copy(mm_i[:, :], mm_f[:, :]).then_inc(dve_step, 1)
            dve.wait_ge(dve_step, 7)
            nc.vector.tensor_scalar(mm_w[:, :], mm_i[:, :], P.bit_length() - 1, None,
                                    ALU.arith_shift_right).then_inc(dve_step, 1)
            dve.wait_ge(dve_step, 8)
            nc.vector.tensor_copy(span_f[:, 0:1], mm_w[:, 0:1]).then_inc(span_f_ready, 1)
            nc.vector.tensor_scalar(span_f[:, 1:2], mm_w[:, 1:2], 1, None, ALU.add).then_inc(span_f_ready, 1)
            dve.wait_ge(span_mm, 1)
            for k in range(2):
                nc.vector.tensor_copy(span_i[0:1, :, k], psTab[0:1, k * P:k * P + C]).then_inc(span_ready, 1)
            dve.sem_inc(onehot_used, S)
            dve.sem_inc(acc_added, 1)
            dve.wait_ge(span_ready, 2)

            visit = dve.alloc_register("dve_visit")
            dve.reg_mov(visit, 0)
            win = [dve.alloc_register("dve_win_lo"), dve.alloc_register("dve_win_hi")]

            def chunk_step(c, p):
                dve.wait_ge(tanh_ready, c + 1)
                nc.vector.tensor_scalar(e_w[:, :], tanh_e[p][:, :], 0.5, 0.5, ALU.mult, ALU.add).then_inc(e_w_ready, 1)
                dve.wait_ge(dst_in[p], 8 * (c - p) + 16)
                nc.vector.tensor_copy(dst_f[:, :], dst_sb[p][:, :]).then_inc(dst_f_ready, 1)
                dve.wait_ge(e_w_ready, c + 2)
                for s in range(S):
                    t = slice(s * T, s * T + T)
                    dve.wait_ge(gathered[s], (c + 1) * (16 * T))
                    nc.vector.tensor_tensor(msg[:, t, 0:D], ring[:, t, :],
                                            e_w[:, t].unsqueeze(2).to_broadcast([P, T, D]),
                                            ALU.mult).then_inc(scaled, 1)
                dve.wait_ge(dst_f_ready, c + 1)
                dve.load(win, span_i[0:1, bass.ds(c, 1), :])
                lo = dve.snap(win[0], min_val=0, max_val=W - 1)
                hi = dve.snap(win[1], min_val=1, max_val=W)
                with dve.Fori(lo, hi, 1) as w:
                    v = dve.snap(visit, min_val=0, max_val=W * C)
                    nc.vector.tensor_scalar(dst_loc[:, :], dst_f[:, :], base_f[:, bass.ds(w, 1)], None,
                                            ALU.subtract).then_inc(loc_ready, 1)
                    dve.wait_ge(loc_ready, v + 1)
                    for s in range(S):
                        t = slice(s * T, s * T + T)
                        dve.wait_ge(onehot_used, v * S + s + 1)
                        nc.vector.tensor_tensor(onehot[:, t, :], iota_f[:, :].unsqueeze(1).to_broadcast([P, T, P]),
                                                dst_loc[:, t].unsqueeze(2).to_broadcast([P, T, P]),
                                                ALU.is_equal).then_inc(onehot_ready, 1)
                    dve.wait_ge(onehot_used, v * S + 2 * S)
                    dve.wait_ge(acc_added, v + 1)
                    aw = acc[:, bass.ds(w, 1), :].rearrange("p o f -> p (o f)")
                    nc.vector.tensor_tensor(aw, aw, psAgg[:, 0:DC], ALU.add).then_inc(acc_added, 1)
                    dve.reg_add(visit, visit, 1)

            chunk_step(0, 0)
            with dve.Fori(1, C - 1, 2) as c:
                chunk_step(c, 1)
                chunk_step(c + 1, 0)

            dve.wait_ge(acc_added, dve.snap(visit, min_val=0, max_val=W * C) + 1)
            nc.vector.tensor_scalar(cnt[:, :], acc[:, :, D], 1.0, None, ALU.max).then_inc(rcnt_ready, 1)
            dve.wait_ge(rcnt_ready, 1)
            nc.vector.reciprocal(rcnt[:, :], cnt[:, :]).then_inc(rcnt_ready, 1)
            dve.wait_ge(rcnt_ready, 2)

            def mean_step(i, p, last=False):
                nw = GL if last else GW
                if not (isinstance(i, int) and i < 2):
                    dve.wait_ge(u_mm, i - 1)
                nc.vector.tensor_tensor(agg_n[p][:, 0:nw, :], acc[:, bass.ds(i * GW, nw), 0:D],
                                        rcnt[:, bass.ds(i * GW, nw)].unsqueeze(2).to_broadcast([P, nw, D]),
                                        ALU.mult).then_inc(agg_ready, 1)

            steps = dve.alloc_register("ln_steps")
            dve.reg_mov(steps, 0)

            def norm_step(i, p, last=False):
                nw = GL if last else GW
                r = res[p]

                def step(ins):
                    ins.then_inc(ln_step, 1)
                    dve.reg_add(steps, steps, 1)
                    dve.wait_ge(ln_step, steps)

                def spread(rows):
                    return rows[:, :].unsqueeze(1).to_broadcast([P, nw, D])

                def statistics(of):
                    for w in range(nw):
                        ins = nc.vector.bn_stats(stats[:, w, :], of(w))
                    ins.then_inc(ln_step, 1)
                    dve.reg_add(steps, steps, 1)
                    dve.wait_ge(w_in, WEIGHTS_IN)
                    dve.wait_ge(ln_step, steps)
                    for w in range(nw):
                        ins = nc.vector.bn_aggr(mv[:, w, :], stats[:, w, :])
                    step(ins)
                    nc.vector.tensor_scalar(var_e[:, 0:nw], mv[:, 0:nw, 1], EPS, None, ALU.add).then_inc(var_ready, 1)

                def normalise(k, of):
                    dve.wait_ge(rstd_ready, i * 2 + k)
                    for w in range(nw):
                        ins = nc.vector.tensor_scalar(r[:, w, :], of(w), mv[:, w, 0:1], rstd[:, w:w + 1],
                                                      ALU.subtract, ALU.mult)
                    return ins

                dve.wait_ge(n_mm, i + 1)
                statistics(lambda w: psN[p][:, w * P:w * P + P])
                if not (isinstance(i, int) and i < 2):
                    dve.wait_ge(res_out[p], 8 * (i - p))
                step(normalise(1, lambda w: psN[p][:, w * P:w * P + P]))
                step(nc.vector.tensor_tensor(r[:, 0:nw, :], r[:, 0:nw, :], spread(g_row), ALU.mult))
                step(nc.vector.tensor_tensor(r[:, 0:nw, :], r[:, 0:nw, :], spread(b_row), ALU.add))
                dve.wait_ge(xo_in[p], (XR0 + 32) if last else 8 * (i - p) + 16)
                step(nc.vector.tensor_tensor(r[:, 0:nw, :], r[:, 0:nw, :], x_in[p][:, 0:nw, :], ALU.add))
                statistics(lambda w: r[:, w, :])
                normalise(2, lambda w: r[:, w, :]).then_inc(res_ready, 1)

            mean_step(0, 0)
            mean_step(1, 1)
            mean_step(2, 0)
            norm_step(0, 0)
            mean_step(3, 1)
            norm_step(1, 1)
            with dve.Fori(4, G - 1, 2) as g:
                mean_step(g, 0)
                norm_step(g - 2, 0)
                mean_step(g + 1, 1)
                norm_step(g - 1, 1)
            mean_step(G, 0, last=True)
            norm_step(G - 2, 0)
            norm_step(G - 1, 1)
            norm_step(G, 0, last=True)


_INS = ['x', 'src', 'dst', 'edge_attr_4', 'L0_gnn_agg_W', 'L0_gnn_agg_b', 'L0_gnn_edge_W1', 'L0_gnn_edge_b1',
        'L0_gnn_edge_W2', 'L0_gnn_edge_b2', 'L0_gnn_upd_W1', 'L0_gnn_upd_b1', 'L0_gnn_upd_W2', 'L0_gnn_upd_b2',
        'L0_gnn_ln_g', 'L0_gnn_ln_b', 'L0_gnn_res_W']


def kernel(**inputs):
    import numpy as _np
    import concourse.bacc as _bacc
    from concourse import mybir as _mybir
    from concourse.bass_utils import run_bass_kernel_spmd as _run

    nc = _bacc.Bacc("TRN2", target_bir_lowering=False, num_devices=1)
    arrays, args = {}, []
    for name in _INS:
        a = _np.ascontiguousarray(inputs[name])
        arrays[f"in_{name}_dram"] = a
        args.append(nc.dram_tensor(f"in_{name}_dram", a.shape, _mybir.dt.from_np(a.dtype), kind="ExternalInput").ap())
    shape = _np.shape(inputs["x"])
    args.append(nc.dram_tensor("out_dram", shape, _mybir.dt.float32, kind="ExternalOutput").ap())
    gnn_layer(nc, *args)
    r = _run(nc, [arrays], core_ids=[0])
    return r.results[0]["out_dram"]
```

```python
from contextlib import ExitStack

import concourse.bass as bass
from concourse import mybir


def gnn_layer(nc, x, src, dst, edge_attr, agg_w, agg_b, edge_w1, edge_b1, edge_w2, edge_b2,
              upd_w1, upd_b1, upd_w2, upd_b2, ln_g, ln_b, res_w, out):
    F32 = mybir.dt.float32
    BF16 = mybir.dt.bfloat16
    I32 = mybir.dt.int32
    ALU = mybir.AluOpType
    ACT = mybir.ActivationFunctionType
    AX = mybir.AxisListType

    P = 128
    N, D = x.shape
    E, A = edge_attr.shape
    J = 25
    C = E // (P * J)
    W = -(-N // P)
    TAIL = N - (W - 1) * P
    GW = 4
    G = W // GW
    GL = W - G * GW
    S = 5
    T = J // S
    Q = [0, 1, 2, 0, 1, 0]
    KB = T * len(Q) * A
    BANKS = [[g + T * b for b in range(GW)] for g in range(T)] + [[20, 21, 22, 23], [24]]
    HG = len(BANKS)
    DC = D + 1
    EPS = 1e-5
    assert C * P * J == E and C % 2 == 1 and G % 2 == 0 and GL == 2 and J % S == 0
    assert S == GW + 1 and J == sum(map(len, BANKS)) and KB <= P

    z_dram = nc.dram_tensor("z_nodes", [N, D], F32).ap()

    src_c = src.rearrange("(c p j) -> c p j", p=P, j=J)
    dst_c = dst.rearrange("(c p j) -> c p j", p=P, j=J)
    dst_rows = dst.rearrange("(c e) -> c e", e=P * J)
    attr_c = edge_attr.rearrange("(c p j) a -> c p (j a)", p=P, j=J)

    def group_rows(t, i):
        return t[bass.ds(i * (GW * P), GW * P), :].rearrange("(w p) f -> p w f", p=P)

    ctx = ExitStack()
    with ctx:
        def sb(name, shape, dt=F32):
            return ctx.enter_context(nc.sbuf_tensor(name, shape, dt))

        def sem(name):
            return ctx.enter_context(nc.semaphore(name))

        ident = sb("ident", [P, P])
        ident_b = sb("ident_b", [P, P], BF16)
        iota_i = sb("iota_i", [P, P], I32)
        iota_f = sb("iota_f", [P, P])
        base_i = sb("base_i", [P, W], I32)
        base_f = sb("base_f", [P, W])
        minus_half = sb("minus_half", [P, GW])
        w_agg = sb("w_agg", [P, D])
        w_u1x = sb("w_u1x", [P, D])
        w_u1a = sb("w_u1a", [P, D])
        w_u2 = sb("w_u2", [P, D])
        w_res = sb("w_res", [P, D])
        w_e1 = sb("w_e1", [A, D])
        w_e1r = [sb(f"w_e1r{k}", [A, D]) for k in range(2)]
        w_e1p = [sb(f"w_e1p{k}", [A, D], BF16) for k in range(3)]
        w_e1q = sb("w_e1q", [len(Q) * A, D], BF16)
        w_e1b = sb("w_e1b", [KB, T, D], BF16)
        w_e2 = sb("w_e2", [P, 1])
        b_agg = sb("b_agg", [P, 1])
        b_e1 = sb("b_e1", [P, 1])
        b_e2 = sb("b_e2", [P, 1])
        b_e2h = sb("b_e2h", [P, 1])
        b_u1 = sb("b_u1", [P, 1])
        b_u2 = sb("b_u2", [P, 1])
        g_row = sb("g_row", [P, D])
        b_row = sb("b_row", [P, D])
        xT = sb("xT", [P, W * P])
        x_in = [sb(f"x_in{p}", [P, GW, D]) for p in range(2)]
        yT = [sb(f"yT{p}", [P, GW * P]) for p in range(2)]
        z_sb = [sb(f"z_sb{p}", [P, GW, D]) for p in range(2)]
        dst_tab = sb("dst_tab", [C, P * J], I32)
        mm_f = sb("mm_f", [C, 2])
        mm_i = sb("mm_i", [C, 2], I32)
        mm_w = sb("mm_w", [C, 2], I32)
        span_f = sb("span_f", [C, 2])
        span_i = sb("span_i", [1, C, 2], I32)
        src_sb = [sb(f"src_sb{p}", [P, J], I32) for p in range(2)]
        dst_sb = [sb(f"dst_sb{p}", [P, J], I32) for p in range(2)]
        attr_sb = [sb(f"attr_sb{p}", [P, J, A]) for p in range(2)]
        attr_r = [sb(f"attr_r{k}", [P, J, A]) for k in range(2)]
        attr_q = [sb(f"attr_q{p}", [P, J, len(Q), A], BF16) for p in range(2)]
        attrT = sb("attrT", [KB, S * P], BF16)
        e_h = [sb(f"e_h{p}", [P, GW * P]) for p in range(2)]
        tanh_e = sb("tanh_e", [P, J])
        e_w = [sb(f"e_w{p}", [P, J]) for p in range(2)]
        dst_f = sb("dst_f", [P, J])
        dst_loc = sb("dst_loc", [P, J])
        ring = sb("ring", [P, J, D])
        msg = [sb(f"msg{p}", [P, J, DC]) for p in range(2)]
        onehot = sb("onehot", [P, J, P])
        acc = sb("acc", [P, W + 1, DC])
        cnt = sb("cnt", [P, W])
        rcnt = sb("rcnt", [P, W])
        agg_n = [msg[p][:, 0:GW, 0:D] for p in range(2)]
        xb = [msg[p][:, GW:2 * GW, 0:D] for p in range(2)]
        ctr = [msg[p][:, 2 * GW:3 * GW, 0:D] for p in range(2)]
        fin = [msg[p][:, 3 * GW:4 * GW, 0:D] for p in range(2)]
        hT = e_h
        res = z_sb
        stats = [[sb(f"stats{k}{p}", [P, GW, 6]) for p in range(2)] for k in range(2)]
        mv = [[sb(f"mv{k}{p}", [P, GW, 2]) for p in range(2)] for k in range(2)]
        var_e = [[sb(f"var_e{k}{p}", [P, GW]) for p in range(2)] for k in range(2)]
        rstd = [[sb(f"rstd{k}{p}", [P, GW]) for p in range(2)] for k in range(2)]
        nbias = [sb(f"nbias{p}", [P, GW]) for p in range(2)]

        banks = [ctx.enter_context(nc.psum_tensor(f"banks{b}", [P, 1024], F32)) for b in range(4)]
        bank = [banks[b // 2][:, (b % 2) * 512:(b % 2) * 512 + 512] for b in range(8)]
        psXT, psA, psZ = bank[0:2], bank[2:4], bank[4:6]
        psAttr, psEw, psHid, psAgg, psTab = bank[0].bitcast(BF16), bank[1], bank[2:4], banks[2], bank[6]
        psU, psH, psN = bank[0:2], bank[2:4], bank[4:6]

        first_in = sem("first_in")
        w_in = sem("w_in")
        w_e1_in = sem("w_e1_in")
        w_e1_split = sem("w_e1_split")
        w_e1q_in = sem("w_e1q_in")
        w_e1b_in = sem("w_e1b_in")
        pool_const = sem("pool_const")
        dve_const = sem("dve_const")
        tab_in = sem("tab_in")
        x_ready = [sem(f"x_ready{p}") for p in range(2)]
        tail_zero = sem("tail_zero")
        xT_mm = sem("xT_mm")
        xT_ready = sem("xT_ready")
        a_mm = sem("a_mm")
        yT_ready = sem("yT_ready")
        z_mm = sem("z_mm")
        z_ready = sem("z_ready")
        z_out = [sem(f"z_out{p}") for p in range(2)]
        tab_step = sem("tab_step")
        span_f_ready = sem("span_f_ready")
        span_mm = sem("span_mm")
        span_ready = sem("span_ready")
        src_in = [sem(f"src_in{p}") for p in range(2)]
        dst_in = [sem(f"dst_in{p}") for p in range(2)]
        attr_in = [sem(f"attr_in{p}") for p in range(2)]
        attr_step = sem("attr_step")
        attr_ready = sem("attr_ready")
        attr_mm = sem("attr_mm")
        attrT_ready = sem("attrT_ready")
        hid_mm = sem("hid_mm")
        e_h_ready = sem("e_h_ready")
        ew_mm = sem("ew_mm")
        tanh_ready = sem("tanh_ready")
        e_w_ready = sem("e_w_ready")
        dst_f_ready = sem("dst_f_ready")
        gathered = [sem(f"gathered{s}") for s in range(S)]
        scaled = sem("scaled")
        loc_ready = sem("loc_ready")
        onehot_ready = sem("onehot_ready")
        onehot_used = sem("onehot_used")
        chunk_used = sem("chunk_used")
        acc_added = sem("acc_added")
        rcnt_ready = sem("rcnt_ready")
        agg_ready = sem("agg_ready")
        xb_ready = sem("xb_ready")
        u_mm = sem("u_mm")
        u_ready = sem("u_ready")
        h_mm = sem("h_mm")
        hT_ready = sem("hT_ready")
        n_mm = sem("n_mm")
        stats_ready = [sem(f"stats_ready{k}") for k in range(2)]
        mv_ready = [sem(f"mv_ready{k}") for k in range(2)]
        var_ready = [sem(f"var_ready{k}") for k in range(2)]
        rstd_ready = [sem(f"rstd_ready{k}") for k in range(2)]
        ctr_ready = sem("ctr_ready")
        r_ready = sem("r_ready")
        nbias_ready = sem("nbias_ready")
        res_ready = sem("res_ready")
        res_out = [sem(f"res_out{p}") for p in range(2)]
        xo_in = [sem(f"xo_in{p}") for p in range(2)]

        FIRST_IN = 16 * 3
        WEIGHTS_IN = 16 * 9
        BEFORE_LAST = 16 * (G // 2)
        LO = G * GW * P

        def small(i, least=2):
            return isinstance(i, int) and i < least

        def over_groups(eng, stages):
            lag = max(k for _, k in stages)
            first = lag + 2 + lag % 2
            for t in range(first):
                for f, k in stages:
                    if t >= k:
                        f(t - k, (t - k) % 2)
            with eng.Fori(first, G - 1, 2) as t:
                for odd in range(2):
                    for f, k in stages:
                        f(t + (odd - k), (odd - k) % 2)
            for t in range(G, G + 1 + lag):
                for f, k in stages:
                    if t - k <= G:
                        f(t - k, (t - k) % 2, *([True] if t - k == G else []))

        block = ctx.enter_context(nc.Block())

        @block.sync
        def _(sp):
            def load_x(i, p, last=False):
                if last:
                    sp.wait_ge(tail_zero, 1)
                    sp.dma_start(x_in[p][:, 0, :], x[LO:LO + P, :]).then_inc(x_ready[p], 16)
                    sp.dma_start(x_in[p][0:TAIL, 1, :], x[LO + P:N, :]).then_inc(x_ready[p], 16)
                    return
                if not small(i):
                    sp.wait_ge(xT_mm, i - 1)
                sp.dma_start(x_in[p][:, :, :], group_rows(x, i)).then_inc(x_ready[p], 16)

            def load_attr(c, p):
                if not small(c):
                    sp.wait_ge(attr_ready, c - 1)
                sp.dma_start(attr_sb[p][:, :, :].rearrange("p j a -> p (j a)"),
                             attr_c[bass.ds(c, 1), :, :].rearrange("o p j -> (o p) j")).then_inc(attr_in[p], 16)

            sp.dma_start(w_agg[:, :], agg_w).then_inc(first_in, 16)
            load_x(0, 0)
            load_x(1, 1)
            load_attr(0, 0)
            load_attr(1, 1)
            for i in range(2, 4):
                load_x(i, i % 2)
            R = C // 8 * 8
            sp.dma_start(dst_tab[0:R, :], dst_rows[0:R, :]).then_inc(tab_in, 16)
            sp.dma_start(dst_tab[R:C, :], dst_rows[R:C, :]).then_inc(tab_in, 16)
            with sp.Fori(4, G - 1, 2) as g:
                load_x(g, 0)
                load_x(g + 1, 1)
            load_x(G, 0, last=True)

            def load_src(c, p):
                if not small(c):
                    sp.wait_ge(scaled, S * (c - 1))
                sp.dma_start(src_sb[p][:, :],
                             src_c[bass.ds(c, 1), :, :].rearrange("o p j -> (o p) j")).then_inc(src_in[p], 16)

            def load_dst(c, p):
                if not small(c):
                    sp.wait_ge(dst_f_ready, c - 1)
                sp.dma_start(dst_sb[p][:, :],
                             dst_c[bass.ds(c, 1), :, :].rearrange("o p j -> (o p) j")).then_inc(dst_in[p], 16)

            for p in range(2):
                load_src(p, p)
                load_dst(p, p)
            load_attr(2, 0)
            load_attr(3, 1)
            with sp.Fori(2, C - 4, 2) as c:
                for p in range(2):
                    load_attr(c + (2 + p), p)
                    load_src(c + p, p)
                    load_dst(c + p, p)
            load_attr(C - 1, 0)
            for c in range(C - 3, C):
                load_src(c, c % 2)
                load_dst(c, c % 2)

            def load_xo(i, p, last=False):
                if not small(i):
                    sp.wait_ge(xb_ready, i - 1)
                if last:
                    sp.dma_start(x_in[p][:, 0, :], x[LO:LO + P, :]).then_inc(xo_in[p], 16)
                    sp.dma_start(x_in[p][0:TAIL, 1, :], x[LO + P:N, :]).then_inc(xo_in[p], 16)
                else:
                    sp.dma_start(x_in[p][:, :, :], group_rows(x, i)).then_inc(xo_in[p], 16)

            def store_res(i, p, last=False):
                sp.wait_ge(res_ready, i + 1)
                if last:
                    sp.dma_start(out[LO:LO + P, :], fin[p][:, 0, :]).then_inc(res_out[p], 16)
                    sp.dma_start(out[LO + P:N, :], fin[p][0:TAIL, 1, :]).then_inc(res_out[p], 16)
                else:
                    sp.dma_start(group_rows(out, i), fin[p][:, :, :]).then_inc(res_out[p], 16)

            sp.wait_ge(xT_mm, G + 1)
            over_groups(sp, [(load_xo, 0), (store_res, 4)])
            sp.wait_ge(res_out[0], BEFORE_LAST + 32)
            sp.wait_ge(res_out[1], BEFORE_LAST)

        @block.gpsimd
        def _(pool):
            nc.gpsimd.memset(ident[:, :], 0.0).then_inc(pool_const, 1)
            pool.wait_ge(pool_const, 1)
            nc.gpsimd.affine_select(out=ident[:, :], in_=ident[:, :], compare_op=ALU.not_equal, fill=1.0, base=0,
                                    pattern=[[-1, P]], channel_multiplier=1).then_inc(pool_const, 1)
            nc.gpsimd.iota(iota_i[:, :], [[1, P]], base=0, channel_multiplier=0).then_inc(pool_const, 1)
            nc.gpsimd.iota(base_i[:, :], [[P, W]], base=0, channel_multiplier=0).then_inc(pool_const, 1)
            nc.gpsimd.memset(minus_half[:, :], -0.5).then_inc(pool_const, 1)
            for p in range(2):
                nc.gpsimd.memset(msg[p][:, :, D:DC], 1.0).then_inc(pool_const, 1)
            nc.gpsimd.memset(acc[:, :, :], 0.0).then_inc(pool_const, 1)
            pool.wait_ge(z_out[0], BEFORE_LAST + 32)
            pool.wait_ge(z_out[1], BEFORE_LAST)
            count = pool.alloc_register("segments_read")
            pool.reg_mov(count, 0)

            def gather_chunk(c, p):
                pool.wait_ge(src_in[p], 8 * (c - p) + 16)
                for s in range(S):
                    if not small(c, 1):
                        pool.reg_add(count, count, 1)
                        pool.wait_ge(pool_const, 5)
                        pool.wait_ge(scaled, count)
                    for j in range(s * T, s * T + T):
                        nc.gpsimd.indirect_dma_start(
                            out=ring[:, j, :], out_offset=None, in_=z_dram[:, :],
                            in_offset=bass.IndirectOffsetOnAxis(ap=src_sb[p][:, j:j + 1], axis=0),
                        ).then_inc(gathered[s], 16)

            gather_chunk(0, 0)
            gather_chunk(1, 1)
            with pool.Fori(2, C - 2, 2) as c:
                gather_chunk(c, 0)
                gather_chunk(c + 1, 1)
            gather_chunk(C - 1, 0)

            def shift_x(i, p, last=False):
                nw = GL if last else GW
                pool.wait_ge(xo_in[p], (BEFORE_LAST + 32) if last else 8 * (i - p) + 16)
                if not small(i):
                    pool.wait_ge(r_ready, i - 1)
                nc.gpsimd.tensor_tensor(xb[p][:, 0:nw, :], x_in[p][:, 0:nw, :],
                                        b_row[:, :].unsqueeze(1).to_broadcast([P, nw, D]),
                                        ALU.add).then_inc(xb_ready, 1)

            def inv_std(k):
                def stage(i, p, last=False):
                    nw = GL if last else GW
                    pool.wait_ge(var_ready[k], i + 1)
                    if k == 1 and not small(i):
                        pool.wait_ge(res_ready, i - 1)
                    nc.gpsimd.tensor_tensor(rstd[k][p][:, 0:nw], var_e[k][p][:, 0:nw], minus_half[:, 0:nw],
                                            ALU.pow).then_inc(rstd_ready[k], 1)
                return stage

            pool.wait_ge(rcnt_ready, 2)
            over_groups(pool, [(inv_std(0), 1), (inv_std(1), 2), (shift_x, 0)])

        @block.scalar
        def _(act):
            act.dma_start(b_agg[:, :], agg_b.rearrange("(p o) -> p o", o=1)).then_inc(first_in, 16)
            act.dma_start(w_u1a[:, :], upd_w1[D:2 * D, :]).then_inc(first_in, 16)
            act.dma_start(w_e1[:, :], edge_w1).then_inc(w_e1_in, 16)
            act.dma_start(b_e2[:, :], edge_b2.rearrange("(o n) -> o n", o=1).to_broadcast([P, 1])).then_inc(w_e1_in, 16)
            for to, of in ((w_u1x[:, :], upd_w1[0:D, :]), (w_u2[:, :], upd_w2), (w_res[:, :], res_w),
                           (w_e2[:, :], edge_w2),
                           (b_e1[:, :], edge_b1.rearrange("(p o) -> p o", o=1)),
                           (b_u1[:, :], upd_b1.rearrange("(p o) -> p o", o=1)),
                           (b_u2[:, :], upd_b2.rearrange("(p o) -> p o", o=1)),
                           (g_row[:, :], ln_g.rearrange("(o n) -> o n", o=1).to_broadcast([P, D])),
                           (b_row[:, :], ln_b.rearrange("(o n) -> o n", o=1).to_broadcast([P, D]))):
                act.dma_start(to, of).then_inc(w_in, 16)
            act.wait_ge(w_e1_split, 5)
            for n, k in enumerate(Q):
                act.dma_start(w_e1q[n * A:n * A + A, :], w_e1p[k][:, :]).then_inc(w_e1q_in, 16)
            act.wait_ge(w_e1q_in, 16 * len(Q))
            for t in range(T):
                r = t * len(Q) * A
                act.dma_start(w_e1b[r:r + len(Q) * A, t, :], w_e1q[:, :]).then_inc(w_e1b_in, 16)
            act.wait_ge(first_in, FIRST_IN)

            def node_step(i, p, last=False):
                n = GL * P if last else GW * P
                act.wait_ge(a_mm, i + 1)
                if not small(i):
                    act.wait_ge(z_mm, i - 1)
                nc.scalar.activation(yT[p][:, 0:n], psA[p][:, 0:n], ACT.Silu, bias=b_agg[:, :]).then_inc(yT_ready, 1)

            def store_z(i, p, last=False):
                act.wait_ge(z_ready, i + 1)
                if last:
                    act.dma_start(z_dram[LO:LO + P, :], z_sb[p][:, 0, :]).then_inc(z_out[p], 16)
                    act.dma_start(z_dram[LO + P:N, :], z_sb[p][0:TAIL, 1, :]).then_inc(z_out[p], 16)
                else:
                    act.dma_start(group_rows(z_dram, i), z_sb[p][:, :, :]).then_inc(z_out[p], 16)

            over_groups(act, [(node_step, 0), (store_z, 2)])
            act.wait_ge(w_in, WEIGHTS_IN)
            act.wait_ge(dve_const, 4)

            def edge_step(c, p):
                later = not small(c, 1)
                act.wait_ge(attr_mm, c + 1)
                if later:
                    act.wait_ge(hid_mm, HG * c)
                nc.scalar.copy(attrT[:, :], psAttr[0:KB, 0:S * P]).then_inc(attrT_ready, 1)
                for g in range(HG):
                    n = len(BANKS[g]) * P
                    act.wait_ge(hid_mm, HG * c + g + 1)
                    if g >= 2:
                        act.wait_ge(ew_mm, HG * c + g - 1)
                    elif later:
                        act.wait_ge(ew_mm, HG * c)
                    nc.scalar.activation(e_h[g % 2][:, 0:n], psHid[g % 2][:, 0:n], ACT.Silu,
                                         bias=b_e1[:, :]).then_inc(e_h_ready, 1)
                act.wait_ge(ew_mm, HG * c + HG)
                nc.scalar.activation(tanh_e[:, :], psEw[:, 0:J], ACT.Tanh, bias=b_e2h[:, :],
                                     scale=0.5).then_inc(tanh_ready, 1)
                act.wait_ge(tanh_ready, c + 1)
                nc.scalar.activation(e_w[p][:, :], tanh_e[:, :], ACT.Copy, bias=0.5, scale=0.5).then_inc(e_w_ready, 1)

            def scale_step(c, p):
                act.wait_ge(e_w_ready, c + 1)
                if not small(c):
                    act.wait_ge(chunk_used, c - 1)
                for s in range(S):
                    act.wait_ge(gathered[s], (c + 1) * (16 * T))
                    for j in range(s * T, s * T + T):
                        ins = nc.scalar.activation(msg[p][:, j, 0:D], ring[:, j, :], ACT.Copy,
                                                   scale=e_w[p][:, j:j + 1])
                    ins.then_inc(scaled, 1)

            edge_step(0, 0)
            edge_step(1, 1)
            scale_step(0, 0)
            edge_step(2, 0)
            scale_step(1, 1)
            with act.Fori(2, C - 2, 2) as c:
                edge_step(c + 1, 1)
                scale_step(c, 0)
                edge_step(c + 2, 0)
                scale_step(c + 1, 1)
            scale_step(C - 1, 0)

            used = act.alloc_register("means_used")
            act.reg_mov(used, 0)

            def mean(i, p, last=False):
                if not small(i):
                    act.reg_add(used, used, 1)
                    act.wait_ge(first_in, FIRST_IN)
                    act.wait_ge(u_mm, used)
                for w in range(GL if last else GW):
                    ins = nc.scalar.activation(agg_n[p][:, w, :],
                                               acc[:, bass.ds(i * GW + w, 1), 0:D].rearrange("p o f -> p (o f)"),
                                               ACT.Copy, scale=rcnt[:, bass.ds(i * GW + w, 1)])
                ins.then_inc(agg_ready, 1)

            def silu_u(i, p, last=False):
                n = GL * P if last else GW * P
                act.wait_ge(u_mm, i + 1)
                if not small(i):
                    act.wait_ge(h_mm, i - 1)
                nc.scalar.activation(yT[p][:, 0:n], psU[p][:, 0:n], ACT.Silu, bias=b_u1[:, :]).then_inc(u_ready, 1)

            def evacuate_h(i, p, last=False):
                n = GL * P if last else GW * P
                act.wait_ge(h_mm, i + 1)
                if not small(i):
                    act.wait_ge(n_mm, i - 1)
                nc.scalar.activation(hT[p][:, 0:n], psH[p][:, 0:n], ACT.Identity, bias=b_u2[:, :]).then_inc(hT_ready, 1)

            def normalise(i, p, last=False):
                act.wait_ge(nbias_ready, i + 1)
                if not small(i):
                    act.wait_ge(res_out[p], 8 * (i - p))
                for w in range(GL if last else GW):
                    ins = nc.scalar.activation(fin[p][:, w, :], res[p][:, w, :], ACT.Identity,
                                               bias=nbias[p][:, w:w + 1], scale=rstd[1][p][:, w:w + 1])
                ins.then_inc(res_ready, 1)

            act.wait_ge(rcnt_ready, 2)
            over_groups(act, [(mean, 0), (silu_u, 1), (evacuate_h, 2), (normalise, 6)])

        @block.tensor
        def _(pe):
            pe.wait_ge(pool_const, 2)
            pe.wait_ge(first_in, FIRST_IN)

            def transpose_x(i, p, last=False):
                pe.wait_ge(x_ready[p], (BEFORE_LAST + 32) if last else 8 * (i - p) + 16)
                if not small(i):
                    pe.wait_ge(xT_ready, i - 1)
                for w in range(GL if last else GW):
                    mm = nc.tensor.transpose(psXT[p][:, w * P:w * P + P], x_in[p][:, w, :], ident[:, :])
                mm.then_inc(xT_mm, 1)

            def project_x(i, p, last=False):
                n = GL * P if last else GW * P
                pe.wait_ge(xT_ready, i + 1)
                if not small(i):
                    pe.wait_ge(yT_ready, i - 1)
                nc.tensor.matmul(psA[p][:, 0:n], w_agg[:, :], xT[:, bass.ds(i * (GW * P), n)],
                                 start=True, stop=True).then_inc(a_mm, 1)

            def make_z(i, p, last=False):
                pe.wait_ge(yT_ready, i + 1)
                if not small(i):
                    pe.wait_ge(z_ready, i - 1)
                for w in range(GL if last else GW):
                    mm = nc.tensor.matmul(psZ[p][:, w * P:w * P + P], yT[p][:, w * P:w * P + P], w_u1a[:, :],
                                          start=True, stop=True)
                mm.then_inc(z_mm, 1)

            over_groups(pe, [(transpose_x, 0), (project_x, 1), (make_z, 2)])

            pe.wait_ge(w_in, WEIGHTS_IN)
            pe.wait_ge(w_e1b_in, 16 * T)
            pe.wait_ge(dve_const, 4)

            def edge_net(c, p):
                later = not small(c, 1)
                pe.wait_ge(attr_ready, c + 1)
                if later:
                    pe.wait_ge(attrT_ready, c)
                for b in range(S):
                    mm = nc.tensor.transpose(psAttr[0:KB, b * P:b * P + P],
                                             attr_q[p][:, b * T:b * T + T, :, :].rearrange("p t q a -> p (t q a)"),
                                             ident_b[:, :])
                mm.then_inc(attr_mm, 1)
                pe.wait_ge(attrT_ready, c + 1)
                if later:
                    pe.wait_ge(e_h_ready, HG * c)

                def hidden(g):
                    to = psHid[g % 2]
                    if g < T:
                        mm = nc.tensor.matmul(to[:, 0:GW * P], w_e1b[:, g, :], attrT[:, 0:GW * P],
                                              start=True, stop=True)
                    else:
                        for n, j in enumerate(BANKS[g]):
                            mm = nc.tensor.matmul(to[:, n * P:n * P + P], w_e1b[:, j % T, :],
                                                  attrT[:, (j // T) * P:(j // T) * P + P], start=True, stop=True)
                    mm.then_inc(hid_mm, 1)

                hidden(0)
                hidden(1)
                if later:
                    pe.wait_ge(tanh_ready, c)
                for g in range(HG):
                    pe.wait_ge(e_h_ready, HG * c + g + 1)
                    for n, j in enumerate(BANKS[g]):
                        mm = nc.tensor.matmul(psEw[:, j:j + 1], e_h[g % 2][:, n * P:n * P + P],
                                              w_e2[:, :], start=True, stop=True)
                    mm.then_inc(ew_mm, 1)
                    if g + 2 < HG:
                        hidden(g + 2)

            visit = pe.alloc_register("pe_visit")
            pe.reg_mov(visit, 0)
            win = [pe.alloc_register("pe_win_lo"), pe.alloc_register("pe_win_hi")]

            def aggregate(c, p):
                pe.wait_ge(scaled, S * c + S)
                pe.load(win, span_i[0:1, bass.ds(c, 1), :])
                lo = pe.snap(win[0], min_val=0, max_val=W - 1)
                hi = pe.snap(win[1], min_val=1, max_val=W)
                with pe.Fori(lo, hi, 1) as w:
                    v = pe.snap(visit, min_val=0, max_val=W * C)
                    pe.wait_ge(acc_added, v + 1)
                    for s in range(S):
                        pe.wait_ge(onehot_ready, v * S + s + 1)
                        for j in range(s * T, s * T + T):
                            mm = nc.tensor.matmul(psAgg[:, bass.ds((v % 2) * 512, DC)], onehot[:, j, :],
                                                  msg[p][:, j, :], start=(j == 0), stop=(j == J - 1))
                        mm.then_inc(onehot_used, 1)
                    pe.reg_add(visit, visit, 1)
                pe.wait_ge(onehot_used, pe.snap(visit, min_val=0, max_val=W * C) * S + S)
                pe.sem_inc(chunk_used, 1)

            edge_net(0, 0)
            edge_net(1, 1)
            pe.wait_ge(span_f_ready, 2)
            for k in range(2):
                mm = nc.tensor.matmul(psTab[0:1, k * P:k * P + C], span_f[:, k:k + 1], ident[0:C, 0:C],
                                      start=True, stop=True)
            mm.then_inc(span_mm, 1)
            pe.wait_ge(span_ready, 2)
            edge_net(2, 0)
            aggregate(0, 0)
            edge_net(3, 1)
            aggregate(1, 1)
            with pe.Fori(3, C - 3, 2) as c:
                edge_net(c + 1, 0)
                aggregate(c - 1, 0)
                edge_net(c + 2, 1)
                aggregate(c, 1)
            edge_net(C - 1, 0)
            aggregate(C - 3, 0)
            aggregate(C - 2, 1)
            aggregate(C - 1, 0)

            def update1(i, p, last=False):
                nw = GL if last else GW
                pe.wait_ge(agg_ready, i + 1)
                if not small(i):
                    pe.wait_ge(u_ready, i - 1)
                nc.tensor.matmul(psU[p][:, 0:nw * P], w_u1x[:, :], xT[:, bass.ds(i * (GW * P), nw * P)],
                                 start=True, stop=False)
                for w in range(nw):
                    mm = nc.tensor.matmul(psU[p][:, w * P:w * P + P], agg_n[p][:, w, :], ident[:, :],
                                          start=False, stop=(w == nw - 1))
                mm.then_inc(u_mm, 1)

            def update2(i, p, last=False):
                nw = GL if last else GW
                pe.wait_ge(u_ready, i + 1)
                if not small(i):
                    pe.wait_ge(hT_ready, i - 1)
                nc.tensor.matmul(psH[p][:, 0:nw * P], w_res[:, :], xT[:, bass.ds(i * (GW * P), nw * P)],
                                 start=True, stop=False)
                nc.tensor.matmul(psH[p][:, 0:nw * P], w_u2[:, :], yT[p][:, 0:nw * P],
                                 start=False, stop=True).then_inc(h_mm, 1)

            def transpose_h(i, p, last=False):
                pe.wait_ge(hT_ready, i + 1)
                if not small(i):
                    pe.wait_ge(ctr_ready, i - 1)
                for w in range(GL if last else GW):
                    mm = nc.tensor.transpose(psN[p][:, w * P:w * P + P], hT[p][:, w * P:w * P + P], ident[:, :])
                mm.then_inc(n_mm, 1)

            over_groups(pe, [(update1, 0), (update2, 1), (transpose_h, 2)])

        @block.vector
        def _(dve):
            nc.vector.memset(w_e1b[:, :, :], 0.0).then_inc(w_e1_split, 1)
            dve.wait_ge(w_e1_in, 32)
            nc.vector.tensor_copy(w_e1p[0][:, :], w_e1[:, :]).then_inc(tab_step, 1)
            dve.wait_ge(tab_step, 1)
            nc.vector.tensor_tensor(w_e1r[0][:, :], w_e1[:, :], w_e1p[0][:, :], ALU.subtract).then_inc(w_e1_split, 1)
            dve.wait_ge(w_e1_split, 2)
            nc.vector.tensor_copy(w_e1p[1][:, :], w_e1r[0][:, :]).then_inc(w_e1_split, 1)
            dve.wait_ge(w_e1_split, 3)
            nc.vector.tensor_tensor(w_e1r[1][:, :], w_e1r[0][:, :], w_e1p[1][:, :],
                                    ALU.subtract).then_inc(w_e1_split, 1)
            dve.wait_ge(w_e1_split, 4)
            nc.vector.tensor_copy(w_e1p[2][:, :], w_e1r[1][:, :]).then_inc(w_e1_split, 1)

            dve.wait_ge(pool_const, 4)
            nc.vector.tensor_copy(ident_b[:, :], ident[:, :]).then_inc(dve_const, 1)
            nc.vector.tensor_copy(iota_f[:, :], iota_i[:, :]).then_inc(dve_const, 1)
            nc.vector.tensor_copy(base_f[:, :], base_i[:, :]).then_inc(dve_const, 1)
            nc.vector.tensor_scalar(b_e2h[:, :], b_e2[:, :], 0.5, None, ALU.mult).then_inc(dve_const, 1)

            def split_attr(c, p):
                a, q = attr_sb[p], attr_q[p]

                def copies(k):
                    return [P, J, k, A]

                dve.wait_ge(attr_in[p], 8 * (c - p) + 16)
                if not small(c):
                    dve.wait_ge(attr_mm, c - 1)
                nc.vector.tensor_copy(q[:, :, 0:3, :], a[:, :, :].unsqueeze(2).to_broadcast(copies(3))).then_inc(attr_step, 1)
                dve.wait_ge(attr_step, c * 4 + 1)
                nc.vector.tensor_tensor(attr_r[0][:, :, :], a[:, :, :], q[:, :, 0, :], ALU.subtract).then_inc(attr_step, 1)
                dve.wait_ge(attr_step, c * 4 + 2)
                nc.vector.tensor_copy(q[:, :, 3:5, :], attr_r[0][:, :, :].unsqueeze(2).to_broadcast(copies(2))).then_inc(attr_step, 1)
                dve.wait_ge(attr_step, c * 4 + 3)
                nc.vector.tensor_tensor(attr_r[1][:, :, :], attr_r[0][:, :, :], q[:, :, 3, :], ALU.subtract).then_inc(attr_step, 1)
                dve.wait_ge(attr_step, c * 4 + 4)
                nc.vector.tensor_copy(q[:, :, 5, :], attr_r[1][:, :, :]).then_inc(attr_ready, 1)

            split_attr(0, 0)
            split_attr(1, 1)

            def evacuate_xT(i, p, last=False):
                n = GL * P if last else GW * P
                if last:
                    nc.vector.memset(x_in[p][:, 1, :], 0.0).then_inc(tail_zero, 1)
                dve.wait_ge(xT_mm, i + 1)
                nc.vector.tensor_copy(xT[:, bass.ds(i * (GW * P), n)], psXT[p][:, 0:n]).then_inc(xT_ready, 1)

            def evacuate_z(i, p, last=False):
                nw = GL if last else GW
                dve.wait_ge(z_mm, i + 1)
                if not small(i):
                    dve.wait_ge(z_out[p], 8 * (i - p))
                nc.vector.tensor_copy(z_sb[p][:, 0:nw, :].rearrange("p w f -> p (w f)"),
                                      psZ[p][:, 0:nw * P]).then_inc(z_ready, 1)

            over_groups(dve, [(evacuate_xT, 0), (evacuate_z, 2)])

            dve.wait_ge(tab_in, 32)
            nc.vector.tensor_reduce(mm_f[:, 0:1], dst_tab[:, :], AX.X, ALU.min).then_inc(tab_step, 1)
            nc.vector.tensor_reduce(mm_f[:, 1:2], dst_tab[:, :], AX.X, ALU.max).then_inc(tab_step, 1)
            dve.wait_ge(tab_step, 3)
            nc.vector.tensor_copy(mm_i[:, :], mm_f[:, :]).then_inc(tab_step, 1)
            dve.wait_ge(tab_step, 4)
            nc.vector.tensor_scalar(mm_w[:, :], mm_i[:, :], P.bit_length() - 1, None,
                                    ALU.arith_shift_right).then_inc(tab_step, 1)
            dve.wait_ge(tab_step, 5)
            nc.vector.tensor_copy(span_f[:, 0:1], mm_w[:, 0:1]).then_inc(span_f_ready, 1)
            nc.vector.tensor_scalar(span_f[:, 1:2], mm_w[:, 1:2], 1, None, ALU.add).then_inc(span_f_ready, 1)
            nc.vector.memset(psAgg[:, 512:512 + DC], 0.0).then_inc(dve_const, 1)
            dve.wait_ge(span_mm, 1)
            for k in range(2):
                nc.vector.tensor_copy(span_i[0:1, :, k], psTab[0:1, k * P:k * P + C]).then_inc(span_ready, 1)
            dve.wait_ge(dve_const, 5)
            dve.wait_ge(pool_const, 8)
            dve.sem_inc(onehot_used, S)
            dve.sem_inc(acc_added, 1)

            visit = dve.alloc_register("dve_visit")
            dve.reg_mov(visit, 0)
            before = dve.alloc_register("dve_window_before")
            dve.reg_mov(before, W)
            win = [dve.alloc_register("dve_win_lo"), dve.alloc_register("dve_win_hi")]

            def add_before(v, own=False):
                window = dve.snap(before, min_val=0, max_val=W)
                to = acc[:, bass.ds(window, 1), :].rearrange("p o f -> p (o f)")
                dve.wait_ge(onehot_used, v * S + S)
                dve.wait_ge(acc_added, v + 1)
                if own:
                    dve.wait_ge(onehot_ready, v * S + S)
                nc.vector.tensor_tensor(to, to, psAgg[:, bass.ds(((v + 1) % 2) * 512, DC)],
                                        ALU.add).then_inc(acc_added, 1)

            def visit_windows(c, p):
                dve.wait_ge(dst_in[p], 8 * (c - p) + 16)
                nc.vector.tensor_copy(dst_f[:, :], dst_sb[p][:, :]).then_inc(dst_f_ready, 1)
                dve.wait_ge(dst_f_ready, c + 1)
                dve.load(win, span_i[0:1, bass.ds(c, 1), :])
                lo = dve.snap(win[0], min_val=0, max_val=W - 1)
                hi = dve.snap(win[1], min_val=1, max_val=W)
                with dve.Fori(lo, hi, 1) as w:
                    v = dve.snap(visit, min_val=0, max_val=W * C)
                    nc.vector.tensor_scalar(dst_loc[:, :], dst_f[:, :], base_f[:, bass.ds(w, 1)], None,
                                            ALU.subtract).then_inc(loc_ready, 1)
                    dve.wait_ge(loc_ready, v + 1)
                    for s in range(S):
                        t = slice(s * T, s * T + T)
                        dve.wait_ge(onehot_used, v * S + s + 1)
                        nc.vector.tensor_tensor(onehot[:, t, :], iota_f[:, :].unsqueeze(1).to_broadcast([P, T, P]),
                                                dst_loc[:, t].unsqueeze(2).to_broadcast([P, T, P]),
                                                ALU.is_equal).then_inc(onehot_ready, 1)
                    add_before(v, own=True)
                    dve.reg_mov(before, w)
                    dve.reg_add(visit, visit, 1)

            split_attr(2, 0)
            split_attr(3, 1)
            dve.wait_ge(span_ready, 2)
            visit_windows(0, 0)
            with dve.Fori(1, C - 5, 2) as c:
                split_attr(c + 3, 0)
                visit_windows(c, 1)
                split_attr(c + 4, 1)
                visit_windows(c + 1, 0)
            split_attr(C - 1, 0)
            for c in range(C - 4, C):
                visit_windows(c, c % 2)
            v = dve.snap(visit, min_val=0, max_val=W * C)
            add_before(v)

            dve.wait_ge(acc_added, v + 2)
            nc.vector.tensor_scalar(cnt[:, :], acc[:, 0:W, D], 1.0, None, ALU.max).then_inc(rcnt_ready, 1)
            dve.wait_ge(rcnt_ready, 1)
            nc.vector.reciprocal(rcnt[:, :], cnt[:, :]).then_inc(rcnt_ready, 1)

            def windows(last):
                return range(GL if last else GW)

            def norm_a(i, p, last=False):
                dve.wait_ge(n_mm, i + 1)
                for w in windows(last):
                    ins = nc.vector.bn_stats(stats[0][p][:, w, :], psN[p][:, w * P:w * P + P])
                ins.then_inc(stats_ready[0], 1)

            def norm_b(i, p, last=False, carry=None):
                dve.wait_ge(rstd_ready[0], i + 1)
                dve.wait_ge(xb_ready, i + 1)
                dve.wait_ge(ctr_ready, i + 1)
                if not small(i):
                    dve.wait_ge(res_ready, i - 1)
                for w in windows(last):
                    if w == windows(last)[-1] and carry:
                        carry()
                    ins = nc.vector.scalar_tensor_tensor(res[p][:, w, :], ctr[p][:, w, :], rstd[0][p][:, w:w + 1],
                                                         xb[p][:, w, :], ALU.mult, ALU.add)
                ins.then_inc(r_ready, 1)

            def aggregate_stats(k, p, last):
                for w in windows(last):
                    ins = nc.vector.bn_aggr(mv[k][p][:, w, :], stats[k][p][:, w, :])
                ins.then_inc(mv_ready[k], 1)

            def variance(k, i, p, last):
                nw = len(windows(last))
                dve.wait_ge(mv_ready[k], i + 1)
                nc.vector.tensor_scalar(var_e[k][p][:, 0:nw], mv[k][p][:, 0:nw, 1], EPS, None,
                                        ALU.add).then_inc(var_ready[k], 1)

            def centre(i, p, last, carry=None):
                for w in windows(last):
                    if w == windows(last)[-1] and carry:
                        carry()
                    ins = nc.vector.scalar_tensor_tensor(ctr[p][:, w, :], psN[p][:, w * P:w * P + P],
                                                         mv[0][p][:, w, 0:1], g_row[:, :], ALU.subtract, ALU.mult)
                ins.then_inc(ctr_ready, 1)

            def stats_b(i, p, last):
                dve.wait_ge(r_ready, i + 1)
                for w in windows(last):
                    ins = nc.vector.bn_stats(stats[1][p][:, w, :], res[p][:, w, :])
                ins.then_inc(stats_ready[1], 1)

            def norm_c(i, p, last):
                nw = len(windows(last))
                dve.wait_ge(rstd_ready[1], i + 1)
                if not small(i):
                    dve.wait_ge(res_ready, i - 1)
                nc.vector.scalar_tensor_tensor(nbias[p][:, 0:nw], mv[1][p][:, 0:nw, 0], -1.0, rstd[1][p][:, 0:nw],
                                               ALU.mult, ALU.mult).then_inc(nbias_ready, 1)

            def norm_step(i, p, last=False):
                a, b, c = small(i, G + 1) or not isinstance(i, int), not small(i, 1), not small(i, 2)
                bl, cl = isinstance(i, int) and i == G + 1, isinstance(i, int) and i == G + 2
                b = b and not cl
                q = 1 - p
                if a:
                    norm_a(i, p, last)
                if c:
                    norm_c(i - 2, p, cl)
                if b:
                    norm_b(i - 1, q, bl, (lambda: dve.wait_ge(stats_ready[0], i + 1)) if a else None)
                elif a:
                    dve.wait_ge(stats_ready[0], i + 1)
                if a:
                    aggregate_stats(0, p, last)
                if b:
                    stats_b(i - 1, q, bl)
                if a:
                    variance(0, i, p, last)
                    centre(i, p, last, (lambda: dve.wait_ge(stats_ready[1], i)) if b else None)
                elif b:
                    dve.wait_ge(stats_ready[1], i)
                if b:
                    aggregate_stats(1, q, bl)
                    variance(1, i - 1, q, bl)

            for i in range(4):
                norm_step(i, i % 2)
            with dve.Fori(4, G - 1, 2) as g:
                norm_step(g, 0)
                norm_step(g + 1, 1)
            norm_step(G, 0, last=True)
            norm_step(G + 1, 1)
            norm_step(G + 2, 0)


_INS = ['x', 'src', 'dst', 'edge_attr_4', 'L0_gnn_agg_W', 'L0_gnn_agg_b', 'L0_gnn_edge_W1', 'L0_gnn_edge_b1',
        'L0_gnn_edge_W2', 'L0_gnn_edge_b2', 'L0_gnn_upd_W1', 'L0_gnn_upd_b1', 'L0_gnn_upd_W2', 'L0_gnn_upd_b2',
        'L0_gnn_ln_g', 'L0_gnn_ln_b', 'L0_gnn_res_W']


def kernel(**inputs):
    import numpy as _np
    import concourse.bacc as _bacc
    from concourse import mybir as _mybir
    from concourse.bass_utils import run_bass_kernel_spmd as _run

    nc = _bacc.Bacc("TRN2", target_bir_lowering=False, num_devices=1)
    arrays, args = {}, []
    for name in _INS:
        a = _np.ascontiguousarray(inputs[name])
        arrays[f"in_{name}_dram"] = a
        args.append(nc.dram_tensor(f"in_{name}_dram", a.shape, _mybir.dt.from_np(a.dtype), kind="ExternalInput").ap())
    shape = _np.shape(inputs["x"])
    args.append(nc.dram_tensor("out_dram", shape, _mybir.dt.float32, kind="ExternalOutput").ap())
    gnn_layer(nc, *args)
    r = _run(nc, [arrays], core_ids=[0])
    return r.results[0]["out_dram"]
```
